# Optimizing a Trainium2 kernel written in Bass

```python
import numpy as np
import jax
import jax.numpy as jnp

def _softmax(x, axis=-1):
    return jax.nn.softmax(x, axis=axis)

def _gelu(x):
    return jax.nn.gelu(x, approximate=True)

def _silu(x):
    return jax.nn.silu(x)

def _sigmoid(x):
    return jax.nn.sigmoid(x)

def _layernorm(x, axis=-1, eps=1e-05):
    m = jnp.mean(x, axis=axis, keepdims=True)
    v = jnp.var(x, axis=axis, keepdims=True)
    return (x - m) / jnp.sqrt(v + eps)

def _scatter_add(tgt, idx, src, axis=0):
    return tgt.at[idx].add(src)

def _segment_sum(src, seg, n):
    return jax.ops.segment_sum(src, seg, n)
kernel_name = 'mk_perceiver_d1_seqx_r4_6521ad'

def setup_inputs(seed: int=0):
    np.random.seed(seed)
    _w = jnp.asarray

    def _rec_inputs():
        import jax
        import jax.numpy as jnp
        _rk = jax.random.key(seed)
        x = -0.0005146 + 1 * jax.random.normal(jax.random.fold_in(_rk, 1), (2, 64, 256), jnp.float32)
        _lenS = 64 - jax.random.randint(jax.random.fold_in(_rk, 7), (2,), 0, max(1, 64 // 4) + 1, jnp.int32)
        _lenS2 = 1024 - jax.random.randint(jax.random.fold_in(_rk, 8), (2,), 0, max(1, 1024 // 4) + 1, jnp.int32)
        _ctx_1024P = jax.random.normal(jax.random.fold_in(_rk, 11), (2, 16, 256), jnp.float32)
        _ctx_1024c = jax.random.dirichlet(jax.random.fold_in(_rk, 511), 0.3 * jnp.ones((16,), jnp.float32), (2, 1024))
        _ctx_1024t = jnp.einsum('bsk,bkd->bsd', _ctx_1024c, _ctx_1024P)
        _ctx_1024t = _ctx_1024t * jax.lax.rsqrt(jnp.mean(jnp.square(_ctx_1024t)) + 1e-12) * 0.953939
        ctx_1024 = -0.000392918 + 0.999932 * (_ctx_1024t + 0.3 * jax.random.normal(jax.random.fold_in(_rk, 611), (2, 1024, 256), jnp.float32))
        _validS = jnp.arange(64)[None, :] < _lenS[:, None]
        _validS2 = jnp.arange(1024)[None, :] < _lenS2[:, None]
        _causal = jnp.tril(jnp.ones((64, 64), dtype=bool))
        mask_BxS2_bf1 = jnp.ones((2, 1024), dtype=bool)
        return (x, ctx_1024, mask_BxS2_bf1)
    x, ctx_1024, mask_BxS2_bf1 = _rec_inputs()

    def _L0_xattn_setup():
        import jax, jax.numpy as jnp
        import numpy as np
        DIM = 256
        DIM_LATENT = 256
        DIM_HEAD = 64
        HEADS = 16
        INNER = HEADS * DIM_HEAD

        def layernorm(x, g, b, eps=1e-05):
            m = jnp.mean(x, axis=-1, keepdims=True)
            v = jnp.mean((x - m) ** 2, axis=-1, keepdims=True)
            return (x - m) / jnp.sqrt(v + eps) * g + b

        def rmsnorm(x, gamma, eps=1e-08):
            n = jnp.linalg.norm(x, axis=-1, keepdims=True) * x.shape[-1] ** (-0.5)
            return x / jnp.maximum(n, eps) * gamma
        key = jax.random.key(seed)
        ks = jax.random.split(key, 8)
        b, n, m = (4, 1024, 128)
        x = jax.random.normal(ks[0], (b, n, DIM), dtype=jnp.float32)
        latents = jax.random.normal(ks[1], (b, m, DIM_LATENT), dtype=jnp.float32)
        mask = jnp.ones((b, n), dtype=bool)
        s = 0.02
        return {'x': x, 'latents': latents, 'mask': mask, 'ln_x_g': jnp.ones((DIM,), jnp.float32), 'ln_x_b': jnp.zeros((DIM,), jnp.float32), 'ln_l_g': jnp.ones((DIM_LATENT,), jnp.float32), 'ln_l_b': jnp.zeros((DIM_LATENT,), jnp.float32), 'qn_g': jnp.ones((DIM_HEAD,), jnp.float32), 'kn_g': jnp.ones((DIM_HEAD,), jnp.float32), 'Wq': jax.random.normal(ks[2], (DIM_LATENT, INNER), jnp.float32) * s, 'Wkv': jax.random.normal(ks[3], (DIM, 2 * INNER), jnp.float32) * s, 'Wout': jax.random.normal(ks[4], (INNER, DIM_LATENT), jnp.float32) * s, 'bout': jnp.zeros((DIM_LATENT,), jnp.float32)}
    _L0_xattn_all = _L0_xattn_setup()
    _L0_xattn_in = {k: v for k, v in _L0_xattn_all.items() if k in ('ln_x_g', 'ln_x_b', 'ln_l_g', 'ln_l_b', 'qn_g', 'kn_g', 'Wq', 'Wkv', 'Wout', 'bout')}
    del _L0_xattn_all

    def _L0_attn_setup():
        import jax, jax.numpy as jnp
        import numpy as np
        SEQ, BATCH, HIDDEN = (512, 2, 256)
        NUM_HEADS, HEAD_DIM = (16, 64)
        LN_EPS = 1e-06
        NEG_INF = -10000000000.0
        key = jax.random.key(seed)
        k1, k2, k3 = jax.random.split(key, 3)
        inputs_q = jax.random.normal(k1, (SEQ, BATCH, HIDDEN), dtype=jnp.float32)
        ln_scale = jnp.ones((HIDDEN,), dtype=jnp.float32)
        ln_bias = jnp.zeros((HIDDEN,), dtype=jnp.float32)
        qkv_kernel = jax.random.normal(k2, (HIDDEN, 3, NUM_HEADS * HEAD_DIM), dtype=jnp.float32) / np.sqrt(HIDDEN).astype(np.float32)
        out_kernel = jax.random.normal(k3, (NUM_HEADS * HEAD_DIM, HIDDEN), dtype=jnp.float32) / np.sqrt(NUM_HEADS * HEAD_DIM).astype(np.float32)
        return {'inputs_q': inputs_q, 'ln_scale': ln_scale, 'ln_bias': ln_bias, 'qkv_kernel': qkv_kernel, 'out_kernel': out_kernel}
    _L0_attn_all = _L0_attn_setup()
    _L0_attn_in = {k: v for k, v in _L0_attn_all.items() if k in ('ln_scale', 'ln_bias', 'qkv_kernel', 'out_kernel')}
    del _L0_attn_all

    def _L0_ffn_setup():
        import jax, jax.numpy as jnp
        import numpy as np
        LN_EPS = 1e-05

        def entmax15(z):
            z = z / 2.0
            z = z - jnp.max(z, axis=-1, keepdims=True)
            zs = -jnp.sort(-z, axis=-1)
            k = jnp.arange(1, z.shape[-1] + 1, dtype=z.dtype)
            mean = jnp.cumsum(zs, axis=-1) / k
            meansq = jnp.cumsum(zs * zs, axis=-1) / k
            ss = k * (meansq - jnp.square(mean))
            delta = (1.0 - ss) / k
            tau = mean - jnp.sqrt(jnp.clip(delta, 0.0))
            support = jnp.sum((tau <= zs).astype(jnp.int32), axis=-1, keepdims=True)
            tau_star = jnp.take_along_axis(tau, support - 1, axis=-1)
            return jnp.square(jnp.clip(z - tau_star, 0.0))

        def layernorm_noaffine(v):
            m = jnp.mean(v, axis=-1, keepdims=True)
            var = jnp.mean(jnp.square(v - m), axis=-1, keepdims=True)
            return (v - m) / jnp.sqrt(var + LN_EPS)

        def cp_mumoe(x, gate, Win, Wout):
            ones = jnp.ones(x.shape[:-1] + (1,), x.dtype)
            xb = jnp.concatenate([x, ones], axis=-1)
            z = jnp.einsum('btd,dr->btr', xb, Win) * gate
            return jnp.einsum('btr,or->bto', z, Wout)
        key = jax.random.key(seed)
        ks = jax.random.split(key, 8)
        B, T, D, O, D2, E, R = (8, 512, 256, 1024, 256, 16, 128)
        s = lambda k, shape, scale: jax.random.normal(k, shape, jnp.float32) * scale
        return {'x': s(ks[0], (B, T, D), 1.0), 'proj': s(ks[1], (D, E), D ** (-0.5)), 'C1': s(ks[2], (E, R), E ** (-0.5)), 'Win1': s(ks[3], (D + 1, R), D ** (-0.5)), 'Wout1': s(ks[4], (O, R), R ** (-0.5)), 'C2': s(ks[5], (E, R), E ** (-0.5)), 'Win2': s(ks[6], (O + 1, R), O ** (-0.5)), 'Wout2': s(ks[7], (D2, R), R ** (-0.5))}
    _L0_ffn_all = _L0_ffn_setup()
    _L0_ffn_in = {k: v for k, v in _L0_ffn_all.items() if k in ('proj', 'C1', 'Win1', 'Wout1', 'C2', 'Win2', 'Wout2')}
    del _L0_ffn_all
    return {'x': x, 'ctx_1024': ctx_1024, 'mask_BxS2_bf1': mask_BxS2_bf1, 'L0_xattn_ln_x_g': _L0_xattn_in['ln_x_g'], 'L0_xattn_ln_x_b': _L0_xattn_in['ln_x_b'], 'L0_xattn_ln_l_g': _L0_xattn_in['ln_l_g'], 'L0_xattn_ln_l_b': _L0_xattn_in['ln_l_b'], 'L0_xattn_qn_g': _L0_xattn_in['qn_g'], 'L0_xattn_kn_g': _L0_xattn_in['kn_g'], 'L0_xattn_Wq': _L0_xattn_in['Wq'], 'L0_xattn_Wkv': _L0_xattn_in['Wkv'], 'L0_xattn_Wout': _L0_xattn_in['Wout'], 'L0_xattn_bout': _L0_xattn_in['bout'], 'L0_attn_ln_scale': _L0_attn_in['ln_scale'], 'L0_attn_ln_bias': _L0_attn_in['ln_bias'], 'L0_attn_qkv_kernel': _L0_attn_in['qkv_kernel'], 'L0_attn_out_kernel': _L0_attn_in['out_kernel'], 'L0_ffn_proj': _L0_ffn_in['proj'], 'L0_ffn_C1': _L0_ffn_in['C1'], 'L0_ffn_Win1': _L0_ffn_in['Win1'], 'L0_ffn_Wout1': _L0_ffn_in['Wout1'], 'L0_ffn_C2': _L0_ffn_in['C2'], 'L0_ffn_Win2': _L0_ffn_in['Win2'], 'L0_ffn_Wout2': _L0_ffn_in['Wout2']}

def reference(x, ctx_1024, mask_BxS2_bf1, L0_xattn_ln_x_g, L0_xattn_ln_x_b, L0_xattn_ln_l_g, L0_xattn_ln_l_b, L0_xattn_qn_g, L0_xattn_kn_g, L0_xattn_Wq, L0_xattn_Wkv, L0_xattn_Wout, L0_xattn_bout, L0_attn_ln_scale, L0_attn_ln_bias, L0_attn_qkv_kernel, L0_attn_out_kernel, L0_ffn_proj, L0_ffn_C1, L0_ffn_Win1, L0_ffn_Wout1, L0_ffn_C2, L0_ffn_Win2, L0_ffn_Wout2):
    import jax
    import jax.numpy as jnp

    def _L0_xattn_ref(x, latents, mask, ln_x_g, ln_x_b, ln_l_g, ln_l_b, qn_g, kn_g, Wq, Wkv, Wout, bout):
        import jax, jax.numpy as jnp
        import numpy as np
        DIM = 256
        DIM_LATENT = 256
        DIM_HEAD = 64
        HEADS = 16
        INNER = HEADS * DIM_HEAD

        def layernorm(x, g, b, eps=1e-05):
            m = jnp.mean(x, axis=-1, keepdims=True)
            v = jnp.mean((x - m) ** 2, axis=-1, keepdims=True)
            return (x - m) / jnp.sqrt(v + eps) * g + b

        def rmsnorm(x, gamma, eps=1e-08):
            n = jnp.linalg.norm(x, axis=-1, keepdims=True) * x.shape[-1] ** (-0.5)
            return x / jnp.maximum(n, eps) * gamma
        b, n, _ = x.shape
        m = latents.shape[1]
        h, d = (HEADS, DIM_HEAD)
        scale = d ** (-0.5)
        xn = layernorm(x, ln_x_g, ln_x_b)
        ln = layernorm(latents, ln_l_g, ln_l_b)
        q = (ln @ Wq).reshape(b, m, h, d).transpose(0, 2, 1, 3)
        kv = jnp.concatenate([xn @ Wkv, ln @ Wkv], axis=1)
        kv = kv.reshape(b, n + m, 2, h, d)
        k = kv[:, :, 0].transpose(0, 2, 1, 3)
        v = kv[:, :, 1].transpose(0, 2, 1, 3)
        qn = rmsnorm(q, qn_g) * scale
        kn = rmsnorm(k, kn_g)
        sim = jnp.einsum('bhid,bhjd->bhij', qn, kn)
        max_neg = -jnp.finfo(sim.dtype).max
        padded_mask = jnp.concatenate([mask, jnp.ones((b, m), bool)], axis=1)
        sim = jnp.where(padded_mask[:, None, None, :], sim, max_neg)
        attn = jax.nn.softmax(sim.astype(jnp.float32), axis=-1).astype(sim.dtype)
        out = jnp.einsum('bhij,bhjd->bhid', attn, v)
        out = out.transpose(0, 2, 1, 3).reshape(b, m, h * d)
        return out @ Wout + bout

    def _L0_attn_ref(inputs_q, ln_scale, ln_bias, qkv_kernel, out_kernel):
        import jax, jax.numpy as jnp
        import numpy as np
        SEQ, BATCH, HIDDEN = (512, 2, 256)
        NUM_HEADS, HEAD_DIM = (16, 64)
        LN_EPS = 1e-06
        NEG_INF = -10000000000.0
        s, b, h = inputs_q.shape
        mu = jnp.mean(inputs_q, axis=-1, keepdims=True)
        var = jnp.mean(jnp.square(inputs_q - mu), axis=-1, keepdims=True)
        ln_out = (inputs_q - mu) * jax.lax.rsqrt(var + LN_EPS) * ln_scale + ln_bias
        qkv = jnp.einsum('sbh,htk->stbk', ln_out, qkv_kernel)
        q = qkv[:, 0].reshape(s, b, NUM_HEADS, HEAD_DIM)
        k = qkv[:, 1].reshape(s, b, NUM_HEADS, HEAD_DIM)
        v = qkv[:, 2].reshape(s, b, NUM_HEADS, HEAD_DIM)
        scale = 1.0 / np.sqrt(HEAD_DIM).astype(np.float32)
        logits = jnp.einsum('qbhd,kbhd->bhqk', q, k) * scale
        causal = jnp.tril(jnp.ones((s, s), dtype=bool))
        logits = jnp.where(causal[None, None], logits, jnp.asarray(NEG_INF, logits.dtype))
        attn = jax.nn.softmax(logits, axis=-1)
        ctx = jnp.einsum('bhqk,kbhd->qbhd', attn, v).reshape(s, b, NUM_HEADS * HEAD_DIM)
        return jnp.einsum('sbk,kh->sbh', ctx, out_kernel)

    def _L0_ffn_ref(x, proj, C1, Win1, Wout1, C2, Win2, Wout2):
        import jax, jax.numpy as jnp
        import numpy as np
        LN_EPS = 1e-05

        def entmax15(z):
            z = z / 2.0
            z = z - jnp.max(z, axis=-1, keepdims=True)
            zs = -jnp.sort(-z, axis=-1)
            k = jnp.arange(1, z.shape[-1] + 1, dtype=z.dtype)
            mean = jnp.cumsum(zs, axis=-1) / k
            meansq = jnp.cumsum(zs * zs, axis=-1) / k
            ss = k * (meansq - jnp.square(mean))
            delta = (1.0 - ss) / k
            tau = mean - jnp.sqrt(jnp.clip(delta, 0.0))
            support = jnp.sum((tau <= zs).astype(jnp.int32), axis=-1, keepdims=True)
            tau_star = jnp.take_along_axis(tau, support - 1, axis=-1)
            return jnp.square(jnp.clip(z - tau_star, 0.0))

        def layernorm_noaffine(v):
            m = jnp.mean(v, axis=-1, keepdims=True)
            var = jnp.mean(jnp.square(v - m), axis=-1, keepdims=True)
            return (v - m) / jnp.sqrt(var + LN_EPS)

        def cp_mumoe(x, gate, Win, Wout):
            ones = jnp.ones(x.shape[:-1] + (1,), x.dtype)
            xb = jnp.concatenate([x, ones], axis=-1)
            z = jnp.einsum('btd,dr->btr', xb, Win) * gate
            return jnp.einsum('btr,or->bto', z, Wout)
        a = entmax15(layernorm_noaffine(jnp.einsum('btd,de->bte', x, proj)))
        g1 = jnp.einsum('bte,er->btr', a, C1)
        h = cp_mumoe(x, g1, Win1, Wout1)
        h = jax.nn.gelu(h, approximate=False)
        g2 = jnp.einsum('bte,er->btr', a, C2)
        return cp_mumoe(h, g2, Win2, Wout2)
    x = x + _L0_xattn_ref(ctx_1024, _layernorm(x, axis=-1), mask_BxS2_bf1, L0_xattn_ln_x_g, L0_xattn_ln_x_b, L0_xattn_ln_l_g, L0_xattn_ln_l_b, L0_xattn_qn_g, L0_xattn_kn_g, L0_xattn_Wq, L0_xattn_Wkv, L0_xattn_Wout, L0_xattn_bout)
    x = x + _L0_attn_ref(_layernorm(x, axis=-1), L0_attn_ln_scale, L0_attn_ln_bias, L0_attn_qkv_kernel, L0_attn_out_kernel)
    x = x + _L0_ffn_ref(_layernorm(x, axis=-1), L0_ffn_proj, L0_ffn_C1, L0_ffn_Win1, L0_ffn_Wout1, L0_ffn_C2, L0_ffn_Win2, L0_ffn_Wout2)
    return x

_drawn_inputs = setup_inputs


def setup_inputs(seed=0):
    import zlib

    import numpy as np

    out = dict(_drawn_inputs(seed))
    spreads = {'L0_xattn_ln_x_g': (1.0, 0.6),
     'L0_xattn_ln_x_b': (0.0, 0.379),
     'L0_xattn_ln_l_g': (1.0, 0.6),
     'L0_xattn_ln_l_b': (0.0, 0.8),
     'L0_xattn_qn_g': (1.0, 0.6),
     'L0_xattn_kn_g': (1.0, 0.6),
     'L0_xattn_bout': (0.0, 0.1),
     'L0_attn_ln_scale': (1.0, 0.2),
     'L0_attn_ln_bias': (0.0, 0.1)}
    factors = {'L0_ffn_proj': 5.316,
     'L0_ffn_C1': 5.294,
     'L0_ffn_Win1': 5.576,
     'L0_ffn_Wout1': 5.562,
     'L0_ffn_C2': 4.936,
     'L0_ffn_Win2': 4.996,
     'L0_ffn_Wout2': 5.228}
    for name, (base, spread) in spreads.items():
        noise = np.random.default_rng([zlib.crc32(name.encode()), seed]).standard_normal(out[name].shape)
        drawn = base * np.exp(spread * noise) if base else spread * noise
        out[name] = jnp.asarray(drawn.astype(out[name].dtype))
    for name, factor in factors.items():
        out[name] = (out[name] * factor).astype(out[name].dtype)
    return out
```

```python
from contextlib import ExitStack

import concourse.bass as bass
from concourse import mybir

F32 = mybir.dt.float32
F32R = mybir.dt.float32r
BF16 = mybir.dt.bfloat16
ACT = mybir.ActivationFunctionType
ALU = mybir.AluOpType
AX = mybir.AxisListType

P = 128
BIG = 3.0e38


def perceiver_layer(nc, x, ctx, mask, ln_x_g, ln_x_b, ln_l_g, ln_l_b, qn_g, kn_g, Wq, Wkv, Wout, bout,
                    ln_scale, ln_bias, qkv_kernel, out_kernel, proj, C1, Win1, Wout1, C2, Win2, Wout2, out):
    B, M, D = x.shape
    J = ctx.shape[1]
    INNER = Wq.shape[1]
    DH = qn_g.shape[0]
    H = INNER // DH
    DC = D // P
    G = H // 2
    NT = J // P
    KW = J + M
    NB = NT + 1
    TILES = B * NT + 1
    UNITS = B * G
    FA = B * NT // 2
    R = C1.shape[1]
    E = proj.shape[1]
    O = Wout1.shape[0]
    OC = O // P
    assert B * M == P and 2 * DH == P and R == P and D == 2 * P and KW == 1088 and B == 2

    x_rows = x.rearrange("b m d -> (b m) d")
    out_rows = out.rearrange("b m d -> (b m) d")
    ctx_tiles = ctx.rearrange("b (t p) d -> (b t) p d", p=P)
    wq_v = Wq.rearrange("(c p) n -> p c n", p=P)
    wkv_v = Wkv.rearrange("(c p) n -> p c n", p=P)
    wout_v = Wout.rearrange("(g p) n -> p g n", p=P)
    qkv_v = qkv_kernel.rearrange("(c p) t n -> p c (t n)", p=P)
    outk_v = out_kernel.rearrange("(g p) n -> p g n", p=P)

    with ExitStack() as stack:
        def sb(name, shape, dt=F32):
            return stack.enter_context(nc.sbuf_tensor(name, shape, dt))

        def sem(name):
            return stack.enter_context(nc.semaphore(name))

        knT = sb("knT", [P, B, G, KW])
        xnh = sb("xnh", [P, B * NT, D], F32R)
        xnl = sb("xnl", [P, B * NT, D], F32R)
        lnh = sb("lnh", [M, B, D], F32R)
        lnl = sb("lnl", [M, B, D], F32R)
        wkh = sb("wkh", [P, DC, INNER], F32R)
        wkl = sb("wkl", [P, DC, INNER], F32R)
        wvh = sb("wvh", [P, DC, INNER], F32R)
        wvl = sb("wvl", [P, DC, INNER], F32R)
        wraw = sb("wraw", [P, DC, INNER])
        sp2 = sb("sp2", [P, 2, KW])
        pth = sb("pth", [P, NB, P], F32R)
        ptl = sb("ptl", [P, NB, P], F32R)
        raw = sb("raw", [P, 4, D])
        xn = sb("xn", [P, 2, D])
        xg = sb("xg", [P, D])
        xth = sb("xth", [P, 2, DC, P], F32R)
        xtl = sb("xtl", [P, 2, DC, P], F32R)
        sk = sb("sk", [P, 2, INNER])
        qbd = sb("qbd", [P, UNITS, P])
        mbias = sb("mbias", [P, B, KW], BF16)
        rows = sb("rows", [P, 3, D])
        oT = sb("oT", [P, G, P])
        xb = sb("xb", [P, D])
        ident = sb("ident", [P, P])
        un = sb("un", [P, D])
        uth = sb("uth", [P, DC, P], F32R)
        utl = sb("utl", [P, DC, P], F32R)
        small = sb("small", [P, 262])
        tsm = sb("tsm", [P, 192])
        warm = sb("warm", [P, 2])

        def early(g, at, width):
            return knT[:, 1, g, at:at + width]

        lat64 = early(0, 0, B * D)[0:M, :].rearrange("p (b d) -> p b d", b=B)
        qsq = early(1, 0, INNER)
        qn = early(2, 0, INNER)
        lnTf = early(3, 0, D).rearrange("p (c r) -> p c r", c=DC)
        lnf = early(3, D, D)
        lat = early(3, 2 * D, D)
        gl = early(4, 0, D)
        bl = early(4, D, D)
        latg = early(4, 2 * D, D)
        wq_sb = knT[:, 1, 5:5 + DC, 0:INNER]
        mask8 = early(7, 0, B * J // 4).bitcast(mybir.dt.uint8).rearrange("p (b j) -> p b j", b=B)

        st = small[:, 0:12].rearrange("p (s n) -> p s n", s=2)
        mv = small[:, 12:20].rearrange("p (s n) -> p s n", s=4)
        ve = small[:, 20:24]
        rstd = small[:, 24:28]
        n2 = small[:, 28:60].rearrange("p (s n) -> p s n", s=2)
        sd = small[:, 60:92].rearrange("p (s n) -> p s n", s=2)
        rn = small[:, 92:124].rearrange("p (s n) -> p s n", s=2)
        nmax = small[:, 124:124 + UNITS]
        rsum = small[:, 140:140 + UNITS]
        rinv = small[:, 156:156 + UNITS]
        mhalf = small[:, 172:188]
        qg = small[:, 188:192]

        lst = small[:, 192:204].rearrange("p (s n) -> p s n", s=2)
        lmv = small[:, 204:208].rearrange("p (s n) -> p s n", s=2)
        lve = small[:, 208:210]
        lrs = small[:, 210:212]
        qn2 = small[:, 212:228]
        qsd = small[:, 228:244]
        qrn = small[:, 244:260]

        b0keys = knT[:, 0, :, :].rearrange("p g n -> p (g n)")
        b1keys = knT[:, 1, :, :].rearrange("p g n -> p (g n)")
        qkv_sb = b0keys[:, 0:DC * 3 * INNER].rearrange("p (c n) -> p c n", c=DC)
        outk_sb = b0keys[:, DC * 3 * INNER:DC * 3 * INNER + G * D].rearrange("p (g n) -> p g n", g=G)
        wout_sb = wraw[:, :, :].rearrange("p c n -> p (c n)").rearrange("p (g n) -> p g n", g=G)
        wout1_sb = sk[:, 0, :].rearrange("p (c r) -> p c r", c=OC)
        win2_sb = sk[:, 1, :].rearrange("p (c r) -> p c r", c=OC)
        wout1T = raw[:, :, :].rearrange("p a n -> p (a n)")
        win1_sb = xn[:, 0, :].rearrange("p (c r) -> p c r", c=DC)
        wout2_sb = xn[:, 1, :].rearrange("p (c r) -> p c r", c=DC)
        wout2T = xg[:, :]
        cw = b0keys[:, 8192:8192 + 2 * R]
        proj_sb = b0keys[:, 8192 + 2 * R:8192 + 2 * R + DC * E].rearrange("p (c e) -> p c e", c=DC)
        tail = {}
        at = 0
        for name, width in (("q2", INNER), ("pr", INNER), ("v2", INNER), ("cT", INNER), ("hg", O), ("t0", D), ("t1", D),
                            ("hT", D), ("hq", D), ("x1", D), ("x2", D), ("z1", P), ("zg", P), ("dm", P), ("sel", M),
                            ("aT", P), ("fo", D)):
            tail[name] = b1keys[:, at:at + width]
            at += width
        assert at <= G * KW

        hT = tail["hT"].rearrange("p (c r) -> p c r", c=DC)
        hq = tail["hq"].rearrange("p (c r) -> p c r", c=DC)

        banks = stack.enter_context(nc.psum_tensor("banks", [P, 8, 512], F32))

        w_x = sem("w_x")
        w_k = [sem("w_k0"), sem("w_k1")]
        w_v = sem("w_v")
        w_q = sem("w_q")
        w_rows = sem("w_rows")
        w_gain = sem("w_gain")
        w_mask = sem("w_mask")
        ones_ready = sem("ones_ready")
        w_lrows = sem("w_lrows")
        z1_ready = sem("z1_ready")
        w_ctx = [sem(f"w_ctx{s}") for s in range(4)]
        w_lat = sem("w_lat")
        consts = sem("consts")
        zeroed = sem("zeroed")
        lat_mv = sem("lat_mv")
        lat_rs = sem("lat_rs")
        lat_hat = sem("lat_hat")
        ln_ready = sem("ln_ready")
        lns_ready = sem("lns_ready")
        dchain = sem("dchain")
        pchain = sem("pchain")
        achain = sem("achain")
        wk_hi = sem("wk_hi")
        wk_lo = sem("wk_lo")
        wv_hi = sem("wv_hi")
        wv_lo = sem("wv_lo")
        mask_ready = sem("mask_ready")
        mv_ready = sem("mv_ready")
        rstd_ready = sem("rstd_ready")
        xhat_ready = sem("xhat_ready")
        xn_ready = sem("xn_ready")
        xnl_ready = sem("xnl_ready")
        xt_ps = sem("xt_ps")
        xth_ready = sem("xth_ready")
        xtl_ready = sem("xtl_ready")
        lnT_ready = sem("lnT_ready")
        k_ps = sem("k_ps")
        sq_ready = sem("sq_ready")
        n2_ready = sem("n2_ready")
        sd_ready = sem("sd_ready")
        rnp_ready = sem("rnp_ready")
        kn_ready = sem("kn_ready")
        kt_ps = sem("kt_ps")
        kt_ready = sem("kt_ready")
        q_ps = sem("q_ps")
        qsq_ready = sem("qsq_ready")
        qn2_ready = sem("qn2_ready")
        qsd_ready = sem("qsd_ready")
        qn_ready = sem("qn_ready")
        qt_ps = sem("qt_ps")
        qg_ready = sem("qg_ready")
        qbd_ready = sem("qbd_ready")
        s_ps = sem("s_ps")
        max_ready = sem("max_ready")
        exp_ready = sem("exp_ready")
        rinv_ready = sem("rinv_ready")
        pt_ps = sem("pt_ps")
        pth_ready = sem("pth_ready")
        ptl_ready = sem("ptl_ready")
        u_ps = sem("u_ps")
        un_ready = sem("un_ready")
        ut_ps = sem("ut_ps")
        uth_ready = sem("uth_ready")
        utl_ready = sem("utl_ready")
        o_ps = sem("o_ps")
        o_ready = sem("o_ready")
        w_tail = {k: sem("w_" + k) for k in ("qkv", "outk", "wout", "rows2", "ffn_a", "ffn_b", "c", "bias")}
        xb_ready = sem("xb_ready")
        t_mv = sem("t_mv")
        t_rs = sem("t_rs")
        y_ps = sem("y_ps")
        x1_ready = sem("x1_ready")
        h_ready = sem("h_ready")
        hT_ps = sem("hT_ps")
        hT_ready = sem("hT_ready")
        q2_ps = sem("q2_ps")
        k2_ps = sem("k2_ps")
        v2_ps = sem("v2_ps")
        q2_ready = sem("q2_ready")
        l_ready = sem("l_ready")
        dsel_ready = sem("dsel_ready")
        dl_ps = sem("dl_ps")
        dl_ready = sem("dl_ready")
        e_ready = sem("e_ready")
        v2_ready = sem("v2_ready")
        w_ready = sem("w_ready")
        cT_ps = sem("cT_ps")
        cT_ready = sem("cT_ready")
        y2_ps = sem("y2_ps")
        x2_ready = sem("x2_ready")
        f_ready = sem("f_ready")
        fT_ps = sem("fT_ps")
        fT_ready = sem("fT_ready")
        e_ps = sem("e_ps")
        z1_ps = sem("z1_ps")
        delta_ready = sem("delta_ready")
        root_ready = sem("root_ready")
        a_ready = sem("a_ready")
        aT_ps = sem("aT_ps")
        aT_ready = sem("aT_ready")
        g_ps = sem("g_ps")
        g_ready = sem("g_ready")
        zg1_ready = sem("zg1_ready")
        h1_ps = sem("h1_ps")
        h1_ready = sem("h1_ready")
        z2_ps = sem("z2_ps")
        zg2_ready = sem("zg2_ready")
        f_ps = sem("f_ps")
        out_ready = sem("out_ready")
        w1T_ps = sem("w1T_ps")
        w1T_ready = sem("w1T_ready")
        ks_ready = sem("ks_ready")
        stored = sem("stored")

        t_st = tsm[:, 0:6]
        t_mvv = tsm[:, 6:8]
        t_ve = tsm[:, 8:9]
        t_rstd = tsm[:, 9:10]
        logit = tsm[:, 10:26]
        dmin = tsm[:, 26:42]
        dneg = tsm[:, 42:58]
        zraw = tsm[:, 58:74]
        zsort = tsm[:, 74:90]
        zrest = tsm[:, 90:106]
        zz = tsm[:, 106:122]
        cs = tsm[:, 122:138]
        cs2 = tsm[:, 138:154]
        kk = tsm[:, 154:170]
        supp = tsm[:, 170:171]
        taus = tsm[:, 171:172]
        bcols = tsm[:, 172:174]
        tmp = tsm[:, 175:191]

        def k_banks(n):
            return 0 if n > FA or n % 2 == 0 else 3

        def t1_bank(n):
            return 5 if n <= FA + 1 else 1

        def t2_bank(n, h):
            return 2 if h == 0 else (5 if n <= FA else 0)

        block = stack.enter_context(nc.Block())
        logits_ps = banks[:, 3:6, :].rearrange("p a n -> p (a n)")[:, 0:KW]

        def row(v):
            return v.rearrange("(a d) -> a d", a=1).to_broadcast([P, D])

        def block_of(u, j):
            return sp2[:, u % 2, j * P:j * P + (P if j < NT else M)], (P if j < NT else M)

        T3 = [(0, 4), (4, 8), (8, NB)]

        @block.sync
        def _(sp):
            sp.dma_start(xb[:, :], x_rows).then_inc(w_x, 16)
            for k in range(B * NT):
                if k >= 4:
                    sp.wait_ge(xn_ready, k - 3)
                sp.dma_start(raw[:, k % 4, :], ctx_tiles[k]).then_inc(w_ctx[k % 4], 16)
                if k == 4:
                    sp.wait_ge(ln_ready, 1)
                    for b in range(B):
                        sp.dma_start(lat64[:, b, :], lnf[b * M:(b + 1) * M, :]).then_inc(w_lat, 16)
                    sp.wait_ge(wk_lo, 2)
                    sp.dma_start(wraw[:, :, :], wkv_v[:, :, INNER:2 * INNER]).then_inc(w_v, 16)
            sp.wait_ge(wv_lo, 1)
            sp.dma_start(wout_sb, wout_v).then_inc(w_tail["wout"], 16)
            sp.wait_ge(s_ps, G)
            sp.dma_start(qkv_sb, qkv_v).then_inc(w_tail["qkv"], 16)
            sp.dma_start(outk_sb, outk_v).then_inc(w_tail["outk"], 16)
            sp.dma_start(cw[0:E, 0:R], C1).then_inc(w_tail["c"], 16)
            sp.dma_start(cw[0:E, R:2 * R], C2).then_inc(w_tail["c"], 16)
            sp.dma_start(proj_sb, proj.rearrange("(c p) e -> p c e", p=P)).then_inc(w_tail["c"], 16)
            sp.wait_ge(kt_ps, 2 * TILES)
            sp.dma_start(wout1_sb, Wout1.rearrange("(c p) r -> p c r", p=P)).then_inc(w_tail["ffn_a"], 16)
            sp.dma_start(win2_sb, Win2[0:O, :].rearrange("(c p) r -> p c r", p=P)).then_inc(w_tail["ffn_b"], 16)
            sp.wait_ge(xt_ps, TILES)
            sp.wait_ge(xnl_ready, B * NT)
            sp.dma_start(win1_sb, Win1[0:D, :].rearrange("(c p) r -> p c r", p=P)).then_inc(w_tail["ffn_b"], 16)
            sp.dma_start(wout2_sb, Wout2.rearrange("(c p) r -> p c r", p=P)).then_inc(w_tail["ffn_a"], 16)
            with nc.allow_non_contiguous_dma(reason="two bias columns"):
                sp.dma_start(bcols[:, 0:1], Win1[D:D + 1, :].rearrange("a r -> r a")).then_inc(w_tail["bias"], 16)
                sp.dma_start(bcols[:, 1:2], Win2[O:O + 1, :].rearrange("a r -> r a")).then_inc(w_tail["bias"], 16)
            sp.dma_start(rows[:, 0, :], row(ln_scale)).then_inc(w_tail["rows2"], 16)
            sp.dma_start(rows[:, 1, :], row(ln_bias)).then_inc(w_tail["rows2"], 16)
            sp.wait_ge(out_ready, 1)
            sp.dma_start(out_rows, tail["fo"]).then_inc(stored, 16)
            sp.wait_ge(stored, 16)

        @block.gpsimd
        def _(pool):
            own = [0]

            def link(ins):
                own[0] += 1
                ins.then_inc(pchain, 1)
                pool.wait_ge(pchain, own[0])

            def rsqrt_var(mean_var, var_eps, dst, eps):
                link(nc.gpsimd.tensor_scalar(var_eps, mean_var[:, 1:2], 1.0, eps, ALU.mult, ALU.add))
                return nc.gpsimd.tensor_tensor(dst, var_eps, mhalf[:, 0:1], ALU.pow)

            def tile_rstd(k):
                pool.wait_ge(mv_ready, k + 1)
                rsqrt_var(mv[:, k % 4, :], ve[:, k % 4:k % 4 + 1], rstd[:, k % 4:k % 4 + 1], 1e-5).then_inc(rstd_ready, 1)

            def tile_norm(k):
                pool.wait_ge(xhat_ready, k + 1)
                if k == 0:
                    pool.wait_ge(w_rows, 48)
                link(nc.gpsimd.tensor_tensor(xg[:, :], raw[:, k % 4, :], rows[:, 0, :], ALU.mult))
                if k >= 2:
                    pool.wait_ge(xt_ps, k)
                nc.gpsimd.tensor_tensor(xn[:, k % 2, :], xg[:, :], rows[:, 1, :], ALU.add).then_inc(xn_ready, 1)
                link(nc.gpsimd.tensor_tensor(xnh[:, k, :], xg[:, :], rows[:, 1, :], ALU.add))
                pool.wait_ge(xn_ready, k + 1)
                nc.gpsimd.tensor_tensor(xnl[:, k, :], xn[:, k % 2, :], xnh[:, k, :].bitcast(F32),
                                        ALU.subtract).then_inc(xnl_ready, 1)

            link(nc.gpsimd.memset(mhalf, -0.5))
            link(nc.gpsimd.memset(ident[:, :], 0.0))
            nc.gpsimd.affine_select(out=ident[:, :], in_=ident[:, :], compare_op=ALU.not_equal, fill=1.0, base=0,
                                    pattern=[[-1, P]], channel_multiplier=1).then_inc(consts, 1)
            for s in range(2):
                pool.wait_ge(lat_mv, s + 1)
                rsqrt_var(lmv[:, s, :], lve[:, s:s + 1], lrs[:, s:s + 1], 1e-5).then_inc(lat_rs, 1)
                tile_rstd(s)
            nc.gpsimd.memset(mbias[:, :, J:KW], 0.0)
            tile_norm(0)
            nc.gpsimd.memset(qbd[:, :, :], 0.0).then_inc(zeroed, 1)
            tile_rstd(2)
            tile_norm(1)
            for n in range(TILES):
                if n > FA:
                    pool.wait_ge(n2_ready, n + 1)
                    nc.gpsimd.tensor_tensor(rn[:, n % 2, :], n2[:, n % 2, :], mhalf, ALU.pow).then_inc(rnp_ready, 1)
                if n + 2 < B * NT:
                    tile_norm(n + 2)
                if n + 3 < B * NT:
                    tile_rstd(n + 3)
                if n == 3:
                    pool.wait_ge(w_gain, 64)
                    link(nc.gpsimd.tensor_tensor(qg[:, 2:3], qg[:, 0:1], qg[:, 1:2], ALU.mult))
                    nc.gpsimd.tensor_scalar(qg[:, 3:4], qg[:, 2:3], DH ** -0.5, 0.0, ALU.mult, ALU.add).then_inc(qg_ready, 1)
                if n == 5:
                    pool.wait_ge(w_lat, 16 * B)
                    link(nc.gpsimd.tensor_copy(lnh[:, :, :], lat64))
                    nc.gpsimd.tensor_tensor(lnl[:, :, :], lat64, lnh[:, :, :].bitcast(F32),
                                            ALU.subtract).then_inc(lns_ready, 1)
            nc.gpsimd.tensor_tensor(xb[:, :], xb[:, :], rows[:, 2, :], ALU.add).then_inc(xb_ready, 1)
            pool.wait_ge(s_ps, UNITS)
            nc.gpsimd.tensor_tensor(tail["dm"][:, 0:M], ident[:, 0:M], ident[:, M:P], ALU.subtract)
            nc.gpsimd.tensor_tensor(tail["dm"][:, M:P], ident[:, M:P], ident[:, 0:M], ALU.subtract)
            nc.gpsimd.tensor_tensor(tail["sel"], ident[:, 0:M], ident[:, M:P], ALU.add).then_inc(dsel_ready, 1)
            nc.gpsimd.iota(kk, pattern=[[1, E]], base=1, channel_multiplier=0,
                           allow_small_or_imprecise_dtypes=True).then_inc(ks_ready, 1)
            for s, eps in enumerate((1e-5, 1e-6, 1e-5, 1e-5)):
                pool.wait_ge(t_mv, s + 1)
                rsqrt_var(t_mvv, t_ve, t_rstd, eps).then_inc(t_rs, 1)

        @block.scalar
        def _(act):
            own = [0]

            def link(ins):
                own[0] += 1
                ins.then_inc(achain, 1)
                act.wait_ge(achain, own[0])

            for h in range(2):
                act.dma_start(wraw[:, :, h * 512:(h + 1) * 512], wkv_v[:, :, h * 512:(h + 1) * 512]).then_inc(w_k[h], 16)
            act.dma_start(rows[:, 0, :], row(ln_x_g)).then_inc(w_rows, 16)
            act.dma_start(rows[:, 1, :], row(ln_x_b)).then_inc(w_rows, 16)
            act.dma_start(gl, row(ln_l_g)).then_inc(w_lrows, 16)
            act.dma_start(bl, row(ln_l_b)).then_inc(w_lrows, 16)
            act.dma_start(rows[:, 2, :], row(bout)).then_inc(w_rows, 16)
            for b in range(B):
                act.dma_start(mask8[:, b, :], mask[b:b + 1, :].to_broadcast([P, J])).then_inc(w_mask, 16)
            act.dma_start(wq_sb, wq_v).then_inc(w_q, 16)
            with nc.allow_non_contiguous_dma(reason="four gain columns"):
                for i, g in enumerate((qn_g, kn_g)):
                    for h in range(2):
                        act.dma_start(qg[h * DH:(h + 1) * DH, i:i + 1], g.rearrange("(d a) -> d a", a=1)).then_inc(w_gain, 16)

            def xt_high(n):
                act.wait_ge(xt_ps, n + 1)
                if n >= 2:
                    act.wait_ge(k_ps, 2 * (n - 1))
                nc.scalar.activation(xth[:, n % 2, :, :], banks[:, t1_bank(n), 0:D].rearrange("p (c r) -> p c r", c=DC),
                                     ACT.Copy).then_inc(xth_ready, 1)

            def squares(n, h):
                act.wait_ge(k_ps, 2 * n + h + 1)
                if n >= 2:
                    act.wait_ge(kt_ps, 2 * (n - 1))
                nc.scalar.activation(sk[:, n % 2, h * 512:(h + 1) * 512], banks[:, k_banks(n) + h, :],
                                     ACT.Square).then_inc(sq_ready, 1)

            def keys_out(n, h):
                act.wait_ge(kt_ps, 2 * n + h + 1)
                bank = banks[:, t2_bank(n, h), :]
                if n == 0:
                    ins = nc.scalar.activation(knT[:, :, 4 * h:4 * h + 4, J:KW],
                                               bank.rearrange("p (g b i) -> p b g i", g=4, b=B), ACT.Copy)
                else:
                    b, t = divmod(n - 1, NT)
                    if n == FA + 1 and h == 0:
                        act.wait_ge(lns_ready, 1)
                        act.wait_ge(mask_ready, 1)
                    ins = nc.scalar.activation(knT[:, b, 4 * h:4 * h + 4, t * P:(t + 1) * P],
                                               bank.rearrange("p (g j) -> p g j", g=4), ACT.Copy)
                ins.then_inc(kt_ready, 1)

            def exponentials(u):
                act.wait_ge(max_ready, u + 1)
                nc.scalar.activation(sp2[:, u % 2, :], sp2[:, u % 2, :], ACT.Exp, bias=nmax[:, u:u + 1], scale=-1.0,
                                     accum_out=rsum[:, u:u + 1]).then_inc(exp_ready, 1)

            def probs_high(u, c):
                j0, j1 = T3[c]
                act.wait_ge(pt_ps, 3 * u + c + 1)
                act.wait_ge(u_ps, u)
                rows_ = block_of(u, j0)[1]
                nc.scalar.activation(pth[0:rows_, j0:j1, :], banks[0:rows_, 6, 0:(j1 - j0) * P].rearrange(
                    "p (j r) -> p j r", j=j1 - j0), ACT.Copy).then_inc(pth_ready, 1)

            def mix_out(u):
                act.wait_ge(u_ps, u + 1)
                act.wait_ge(rinv_ready, u + 1)
                act.wait_ge(ut_ps, u)
                nc.scalar.activation(un[:, :], banks[:, 7, 0:D], ACT.Copy, scale=rinv[:, u:u + 1]).then_inc(un_ready, 1)

            def mixT_high(u):
                act.wait_ge(ut_ps, u + 1)
                act.wait_ge(o_ps, u)
                nc.scalar.activation(uth[:, :, :], banks[:, 7, D:2 * D].rearrange("p (c r) -> p c r", c=DC),
                                     ACT.Copy).then_inc(uth_ready, 1)

            def heads_out(u):
                b, g = divmod(u, G)
                act.wait_ge(o_ps, u + 1)
                for h in range(2):
                    last = nc.scalar.activation(oT[h * DH:(h + 1) * DH, g, b * M:(b + 1) * M],
                                                banks[h * DH:(h + 1) * DH, 7, h * M:(h + 1) * M], ACT.Copy)
                last.then_inc(o_ready, 1)

            def wk_high(h):
                act.wait_ge(w_k[h], 16)
                cols = slice(h * 512, (h + 1) * 512)
                nc.scalar.activation(wkh[:, :, cols], wraw[:, :, cols], ACT.Copy).then_inc(wk_hi, 1)

            act.wait_ge(ones_ready, 1)
            nc.scalar.activation(warm[:, 1:2], warm[:, 0:1], ACT.Sqrt)
            wk_high(0)
            xt_high(0)
            wk_high(1)
            nc.scalar.activation(lnTf, banks[:, t1_bank(0), 0:D].rearrange("p (c r) -> p c r", c=DC),
                                 ACT.Copy).then_inc(lnT_ready, 1)
            for n in range(FA + 1):
                xt_high(n + 1)
                squares(n, 0)
                squares(n, 1)
                if n == 2:
                    for h in range(2):
                        act.wait_ge(q_ps, h + 1)
                        nc.scalar.activation(qsq[:, h * 512:(h + 1) * 512], banks[:, 6 + h, :], ACT.Square).then_inc(qsq_ready, 1)
                if n == 3:
                    act.wait_ge(qn2_ready, 1)
                    nc.scalar.activation(qsd, qn2, ACT.Sqrt).then_inc(qsd_ready, 1)
                if n == 5:
                    act.wait_ge(qg_ready, 1)
                    act.wait_ge(zeroed, 1)
                    pairs = qbd[:, :, :].rearrange("p (b g) i -> p b g i", b=B)
                    for h in range(2):
                        act.wait_ge(qt_ps, h + 1)
                        for e in range(2):
                            e0, e1 = e * DH, (e + 1) * DH
                            last = nc.scalar.activation(
                                pairs[e0:e1, :, 4 * h:4 * h + 4, e * M:(e + 1) * M],
                                banks[e0:e1, 6 + h, :].rearrange("p (g b i) -> p b g i", g=4, b=B),
                                ACT.Copy, scale=qg[e0:e1, 3:4])
                    last.then_inc(qbd_ready, 1)
                act.wait_ge(n2_ready, n + 1)
                nc.scalar.activation(sd[:, n % 2, :], n2[:, n % 2, :], ACT.Sqrt).then_inc(sd_ready, 1)
                if n >= 1:
                    keys_out(n - 1, 0)
                    keys_out(n - 1, 1)
            keys_out(FA, 0)
            keys_out(FA, 1)
            act.wait_ge(w_v, 16)
            nc.scalar.activation(wvh[:, :, :], wraw[:, :, :], ACT.Copy).then_inc(wv_hi, 1)
            exponentials(0)
            for u in range(UNITS):
                n = FA + 1 + u
                if u == 0:
                    squares(n, 0)
                    squares(n, 1)
                else:
                    mix_out(u - 1)
                probs_high(u, 0)
                if 0 < u and n < TILES:
                    squares(n, 0)
                if u > 0:
                    mixT_high(u - 1)
                if 0 < u and n < TILES:
                    squares(n, 1)
                probs_high(u, 1)
                if u > 0:
                    heads_out(u - 1)
                probs_high(u, 2)
                if u + 1 < UNITS and u != G - 1:
                    exponentials(u + 1)
                if n + 1 < TILES:
                    xt_high(n + 1)
                if n < TILES:
                    keys_out(n, 0)
                    keys_out(n, 1)
                if u == G - 1:
                    exponentials(u + 1)
                if u == UNITS - 2:
                    act.wait_ge(w1T_ps, 1)
                    nc.scalar.activation(wout1T, banks[:, 0:2, :].rearrange("p a n -> p (a n)"), ACT.Copy)
                    nc.scalar.activation(wout2T, banks[:, 2, 0:D], ACT.Copy).then_inc(w1T_ready, 1)
            mix_out(UNITS - 1)
            mixT_high(UNITS - 1)
            heads_out(UNITS - 1)

            act.wait_ge(hT_ps, 1)
            act.wait_ge(s_ps, UNITS)
            hps = banks[:, 1, 0:D].rearrange("p (c r) -> p c r", c=DC)
            nc.scalar.activation(hT, hps, ACT.Copy)
            for e in range(2):
                last = nc.scalar.activation(hq[:, :, e * M:(e + 1) * M], hps[:, :, M:P], ACT.Copy)
            last.then_inc(hT_ready, 1)
            act.wait_ge(q2_ps, 1)
            nc.scalar.activation(tail["q2"], banks[:, 4:6, :].rearrange("p a n -> p (a n)"), ACT.Copy).then_inc(q2_ready, 1)
            for i, src in enumerate((dmin, dneg)):
                act.wait_ge(dl_ready, i + 1)
                nc.scalar.activation(src, src, ACT.Exp, scale=DH ** -0.5).then_inc(e_ready, 1)
            act.wait_ge(v2_ps, 1)
            nc.scalar.activation(tail["v2"][0:M, :], banks[0:M, 6:8, :].rearrange("p a n -> p (a n)"), ACT.Copy).then_inc(v2_ready, 1)
            act.wait_ge(cT_ps, 1)
            nc.scalar.activation(tail["cT"], banks[:, 2:4, :].rearrange("p a n -> p (a n)"), ACT.Copy).then_inc(cT_ready, 1)
            act.wait_ge(fT_ps, 1)
            nc.scalar.activation(tail["hT"], banks[:, 1, 0:D], ACT.Copy).then_inc(fT_ready, 1)
            act.wait_ge(z1_ps, 1)
            act.wait_ge(w_tail["bias"], 32)
            nc.scalar.activation(tail["z1"], banks[:, 3, 0:P], ACT.Identity, bias=bcols[:, 0:1]).then_inc(z1_ready, 1)
            act.wait_ge(delta_ready, 1)
            nc.scalar.activation(cs2, cs2, ACT.Sqrt).then_inc(root_ready, 1)
            act.wait_ge(aT_ps, 1)
            nc.scalar.activation(tail["aT"][0:E, :], banks[0:E, 4, 0:P], ACT.Copy).then_inc(aT_ready, 1)
            act.wait_ge(g_ps, 2)
            nc.scalar.activation(tail["zg"], banks[:, 6, 0:P], ACT.Copy).then_inc(g_ready, 1)
            for h in range(2):
                act.wait_ge(h1_ps, h + 1)
                nc.scalar.activation(tail["hg"][:, h * 512:(h + 1) * 512], banks[:, h, :], ACT.Gelu).then_inc(h1_ready, 1)

        @block.vector
        def _(dve):
            own = [0]

            def link(ins):
                own[0] += 1
                ins.then_inc(dchain, 1)
                dve.wait_ge(dchain, own[0])

            def stats(src, dst, tmp6):
                link(nc.vector.bn_stats(tmp6, src))
                return nc.vector.bn_aggr(dst, tmp6)

            def center(dst, src, mean, rs):
                return nc.vector.tensor_scalar(dst, src, mean, rs, ALU.subtract, ALU.mult)

            def tile_stats(k):
                dve.wait_ge(w_ctx[k % 4], 16 * (k // 4 + 1))
                if k >= 4:
                    dve.wait_ge(xhat_ready, k - 3)
                stats(raw[:, k % 4, :], mv[:, k % 4, :], st[:, k % 2, :]).then_inc(mv_ready, 1)

            def tile_center(k):
                dve.wait_ge(rstd_ready, k + 1)
                center(raw[:, k % 4, :], raw[:, k % 4, :], mv[:, k % 4, 0:1], rstd[:, k % 4:k % 4 + 1]).then_inc(xhat_ready, 1)

            def xt_low(n):
                dve.wait_ge(xth_ready, n + 1)
                if n == 0:
                    dve.wait_ge(lnT_ready, 1)
                nc.vector.tensor_tensor(xtl[:, n % 2, :, :], banks[:, t1_bank(n), 0:D].rearrange("p (c r) -> p c r", c=DC),
                                        xth[:, n % 2, :, :].bitcast(F32), ALU.subtract).then_inc(xtl_ready, 1)

            def key_norm2(n, h):
                dve.wait_ge(sq_ready, 2 * n + h + 1)
                link(nc.vector.tensor_reduce(n2[:, n % 2, 8 * h:8 * h + 8],
                                             sk[:, n % 2, h * 512:(h + 1) * 512].rearrange("p (h d) -> p h d", d=DH),
                                             AX.X, ALU.add))

            def key_clamp(n):
                nc.vector.tensor_scalar(n2[:, n % 2, :], n2[:, n % 2, :], 1.0 / DH, 1e-16, ALU.mult, ALU.max).then_inc(n2_ready, 1)

            def key_scale(n, h):
                if n > FA:
                    dve.wait_ge(rnp_ready, n - FA)
                nc.vector.tensor_tensor(
                    sk[:, n % 2, h * 512:(h + 1) * 512].rearrange("p (h d) -> p h d", d=DH),
                    banks[:, k_banks(n) + h, :].rearrange("p (h d) -> p h d", d=DH),
                    rn[:, n % 2, 8 * h:8 * h + 8].to_broadcast([P, 8, DH]), ALU.mult).then_inc(kn_ready, 1)

            def logits_max(u):
                dve.wait_ge(s_ps, u + 1)
                if u == 0:
                    dve.wait_ge(mask_ready, 1)
                if u >= 2:
                    dve.wait_ge(pt_ps, 3 * (u - 1))
                nc.vector.tensor_tensor_reduce(out=sp2[:, u % 2, :], in0=logits_ps, in1=mbias[:, u // G, :], scale=-1.0,
                                               scalar=BIG, op0=ALU.add, op1=ALU.min,
                                               accum_out=nmax[:, u:u + 1]).then_inc(max_ready, 1)

            def inverse_sum(u):
                dve.wait_ge(exp_ready, u + 1)
                nc.vector.reciprocal(rinv[:, u:u + 1], rsum[:, u:u + 1]).then_inc(rinv_ready, 1)

            def probs_low(u, c):
                j0, j1 = T3[c]
                rows_ = block_of(u, j0)[1]
                dve.wait_ge(pth_ready, 3 * u + c + 1)
                nc.vector.tensor_tensor(ptl[0:rows_, j0:j1, :], banks[0:rows_, 6, 0:(j1 - j0) * P].rearrange(
                    "p (j r) -> p j r", j=j1 - j0), pth[0:rows_, j0:j1, :].bitcast(F32), ALU.subtract).then_inc(ptl_ready, 1)

            def mixT_low(u):
                dve.wait_ge(uth_ready, u + 1)
                nc.vector.tensor_tensor(utl[:, :, :], banks[:, 7, D:2 * D].rearrange("p (c r) -> p c r", c=DC),
                                        uth[:, :, :].bitcast(F32), ALU.subtract).then_inc(utl_ready, 1)

            nc.vector.memset(warm[:, 0:1], 1.0).then_inc(ones_ready, 1)
            dve.wait_ge(w_x, 16)
            stats(xb[:, :], lmv[:, 0, :], lst[:, 0, :]).then_inc(lat_mv, 1)
            dve.wait_ge(lat_mv, 1)
            tile_stats(0)
            dve.wait_ge(lat_rs, 1)
            link(center(lat, xb[:, :], lmv[:, 0, 0:1], lrs[:, 0:1]))
            stats(lat, lmv[:, 1, :], lst[:, 1, :]).then_inc(lat_mv, 1)
            dve.wait_ge(lat_mv, 2)
            tile_stats(1)
            dve.wait_ge(lat_rs, 2)
            dve.wait_ge(w_lrows, 32)
            link(nc.vector.scalar_tensor_tensor(latg, lat, lmv[:, 1, 0:1], gl, ALU.subtract, ALU.mult))
            nc.vector.scalar_tensor_tensor(lnf, latg, lrs[:, 1:2], bl, ALU.mult, ALU.add).then_inc(ln_ready, 1)
            tile_center(0)
            def wk_low(h):
                dve.wait_ge(wk_hi, h + 1)
                cols = slice(h * 512, (h + 1) * 512)
                nc.vector.tensor_tensor(wkl[:, :, cols], wraw[:, :, cols], wkh[:, :, cols].bitcast(F32),
                                        ALU.subtract).then_inc(wk_lo, 1)

            wk_low(0)
            xt_low(0)
            wk_low(1)
            tile_stats(2)
            tile_center(1)
            for n in range(FA + 1):
                xt_low(n + 1)
                tile_center(n + 2)
                key_norm2(n, 0)
                key_norm2(n, 1)
                key_clamp(n)
                tile_stats(n + 3)
                if n == 3:
                    for h in range(2):
                        dve.wait_ge(qsq_ready, h + 1)
                        link(nc.vector.tensor_reduce(qn2[:, 8 * h:8 * h + 8], qsq[:, h * 512:(h + 1) * 512].rearrange(
                            "p (h d) -> p h d", d=DH), AX.X, ALU.add))
                    nc.vector.tensor_scalar(qn2, qn2, 1.0 / DH, 1e-16, ALU.mult, ALU.max).then_inc(qn2_ready, 1)
                if n == 4:
                    dve.wait_ge(qsd_ready, 1)
                    link(nc.vector.reciprocal(qrn, qsd))
                    for h in range(2):
                        nc.vector.tensor_tensor(
                            qn[:, h * 512:(h + 1) * 512].rearrange("p (h d) -> p h d", d=DH),
                            banks[:, 6 + h, :].rearrange("p (h d) -> p h d", d=DH),
                            qrn[:, 8 * h:8 * h + 8].to_broadcast([P, 8, DH]), ALU.mult).then_inc(qn_ready, 1)
                dve.wait_ge(sd_ready, n + 1)
                link(nc.vector.reciprocal(rn[:, n % 2, :], sd[:, n % 2, :]))
                key_scale(n, 0)
                key_scale(n, 1)
                if n == 1:
                    dve.wait_ge(w_mask, 32)
                    nc.vector.tensor_scalar(mbias[:, :, 0:J], mask8, 1.0, BIG, ALU.subtract, ALU.mult).then_inc(mask_ready, 1)
            logits_max(0)
            dve.wait_ge(wv_hi, 1)
            nc.vector.tensor_tensor(wvl[:, :, :], wraw[:, :, :], wvh[:, :, :].bitcast(F32), ALU.subtract).then_inc(wv_lo, 1)
            inverse_sum(0)
            for u in range(UNITS):
                n = FA + 1 + u
                keys = n < TILES
                if keys and u == 0:
                    key_norm2(n, 0)
                    key_norm2(n, 1)
                    key_clamp(n)
                probs_low(u, 0)
                if keys and u > 0:
                    key_norm2(n, 0)
                if u > 0:
                    mixT_low(u - 1)
                if keys and u > 0:
                    key_norm2(n, 1)
                    key_clamp(n)
                probs_low(u, 1)
                if keys and n + 2 < B * NT:
                    tile_center(n + 2)
                if u + 1 < UNITS and u != G - 1 and not keys:
                    logits_max(u + 1)
                probs_low(u, 2)
                if u + 1 < UNITS and u != G - 1 and keys:
                    logits_max(u + 1)
                if keys and n + 3 < B * NT:
                    tile_stats(n + 3)
                if keys:
                    key_scale(n, 0)
                    key_scale(n, 1)
                if n + 1 < TILES:
                    xt_low(n + 1)
                if u == G - 1:
                    logits_max(u + 1)
                if u + 1 < UNITS:
                    inverse_sum(u + 1)
            mixT_low(UNITS - 1)

            def norm(s, src, dst):
                stats(src, t_mvv, t_st).then_inc(t_mv, 1)
                dve.wait_ge(t_rs, s + 1)
                return center(dst, src, t_mvv[:, 0:1], t_rstd)

            dve.wait_ge(y_ps, 1)
            dve.wait_ge(xb_ready, 1)
            nc.vector.tensor_tensor(tail["x1"], banks[:, 0, 0:D], xb[:, :], ALU.add).then_inc(x1_ready, 1)
            dve.wait_ge(x1_ready, 1)
            link(norm(0, tail["x1"], tail["t0"]))
            stats(tail["t0"], t_mvv, t_st).then_inc(t_mv, 1)
            dve.wait_ge(t_rs, 2)
            dve.wait_ge(w_tail["rows2"], 32)
            link(nc.vector.scalar_tensor_tensor(tail["t1"], tail["t0"], t_mvv[:, 0:1], rows[:, 0, :], ALU.subtract, ALU.mult))
            nc.vector.scalar_tensor_tensor(tail["t0"], tail["t1"], t_rstd, rows[:, 1, :], ALU.mult, ALU.add).then_inc(h_ready, 1)

            dve.wait_ge(q2_ready, 1)
            dve.wait_ge(k2_ps, 1)
            link(nc.vector.tensor_tensor(tail["pr"], banks[:, 2:4, :].rearrange("p a n -> p (a n)"), tail["q2"], ALU.mult))
            nc.vector.tensor_reduce(logit, tail["pr"].rearrange("p (h d) -> p h d", d=DH), AX.X, ALU.add).then_inc(l_ready, 1)
            dve.wait_ge(dl_ps, 1)
            nc.vector.tensor_scalar(dmin, banks[:, 1, D:D + H], 0.0, None, ALU.min).then_inc(dl_ready, 1)
            nc.vector.tensor_scalar(dneg, banks[:, 1, D:D + H], -1.0, 0.0, ALU.mult, ALU.min).then_inc(dl_ready, 1)
            dve.wait_ge(e_ready, 2)
            link(nc.vector.tensor_tensor(tmp, dmin, dneg, ALU.add))
            link(nc.vector.reciprocal(dneg, tmp))
            link(nc.vector.tensor_tensor(dmin, dmin, dneg, ALU.mult))
            dve.wait_ge(v2_ready, 1)
            nc.vector.tensor_tensor(tail["pr"].rearrange("p (h d) -> p h d", d=DH),
                                    banks[:, 6:8, :].rearrange("p a (h d) -> p (a h) d", d=DH),
                                    dmin.to_broadcast([P, H, DH]), ALU.mult).then_inc(w_ready, 1)
            dve.wait_ge(y2_ps, 1)
            nc.vector.tensor_tensor(tail["x2"], banks[:, 0, 0:D], tail["x1"], ALU.add).then_inc(x2_ready, 1)
            dve.wait_ge(x2_ready, 1)
            norm(2, tail["x2"], tail["t0"]).then_inc(f_ready, 1)

            dve.wait_ge(e_ps, 1)
            link(norm(3, banks[:, 2, 0:E], zraw))
            link(nc.vector.max(zsort[:, 0:8], zraw))
            link(nc.vector.match_replace(zrest, zsort[:, 0:8], zraw, -BIG))
            link(nc.vector.max(zsort[:, 8:16], zrest))
            link(nc.vector.tensor_scalar(zz, zraw, zsort[:, 0:1], 0.5, ALU.subtract, ALU.mult))
            link(nc.vector.tensor_scalar(zrest, zsort, zsort[:, 0:1], 0.5, ALU.subtract, ALU.mult))
            zs = zrest
            link(nc.vector.tensor_tensor(tmp, zs, zs, ALU.mult))
            link(nc.vector.memset(zraw, 1.0))
            link(nc.vector.tensor_tensor_scan(cs, zraw, zs, 0.0, ALU.mult, ALU.add))
            link(nc.vector.tensor_tensor_scan(cs2, zraw, tmp, 0.0, ALU.mult, ALU.add))
            dve.wait_ge(ks_ready, 1)
            link(nc.vector.reciprocal(zsort, kk))
            link(nc.vector.tensor_tensor(cs, cs, zsort, ALU.mult))
            link(nc.vector.tensor_tensor(cs2, cs2, zsort, ALU.mult))
            link(nc.vector.tensor_tensor(tmp, cs, cs, ALU.mult))
            link(nc.vector.tensor_tensor(cs2, cs2, tmp, ALU.subtract))
            link(nc.vector.tensor_tensor(cs2, cs2, kk, ALU.mult))
            link(nc.vector.tensor_scalar(cs2, cs2, -1.0, 1.0, ALU.mult, ALU.add))
            link(nc.vector.tensor_tensor(cs2, cs2, zsort, ALU.mult))
            nc.vector.tensor_scalar(cs2, cs2, 0.0, None, ALU.max).then_inc(delta_ready, 1)
            dve.wait_ge(root_ready, 1)
            link(nc.vector.tensor_tensor(cs, cs, cs2, ALU.subtract))
            link(nc.vector.tensor_tensor(tmp, cs, zs, ALU.is_le))
            link(nc.vector.tensor_reduce(supp, tmp, AX.X, ALU.add))
            link(nc.vector.scalar_tensor_tensor(tmp, kk, supp, cs, ALU.is_equal, ALU.mult))
            link(nc.vector.tensor_reduce(taus, tmp, AX.X, ALU.add))
            link(nc.vector.tensor_scalar(zz, zz, taus, 0.0, ALU.subtract, ALU.max))
            nc.vector.tensor_tensor(zz, zz, zz, ALU.mult).then_inc(a_ready, 1)
            dve.wait_ge(z1_ready, 1)
            dve.wait_ge(g_ps, 1)
            nc.vector.tensor_tensor(tail["z1"], banks[:, 5, 0:P], tail["z1"], ALU.mult).then_inc(zg1_ready, 1)
            dve.wait_ge(z2_ps, 1)
            dve.wait_ge(g_ready, 1)
            nc.vector.scalar_tensor_tensor(tail["zg"], banks[:, 3, 0:P], bcols[:, 1:2], tail["zg"], ALU.add,
                                           ALU.mult).then_inc(zg2_ready, 1)
            dve.wait_ge(f_ps, 1)
            nc.vector.tensor_tensor(tail["fo"], banks[:, 2, 0:D], tail["x2"], ALU.add).then_inc(out_ready, 1)

        @block.tensor
        def _(pe):
            def transposes(dst, src, count, width=P, rows_=P):
                for i in range(count):
                    last = nc.tensor.transpose(dst[0:width, i * P:i * P + rows_], src(i), ident[0:rows_, 0:rows_])
                return last

            def norm_transposed(n):
                if n == 0:
                    pe.wait_ge(consts, 1)
                    pe.wait_ge(ln_ready, 1)
                    src = lnf
                else:
                    pe.wait_ge(xn_ready, n)
                    src = xn[:, (n - 1) % 2, :]
                if n == 1:
                    pe.wait_ge(xtl_ready, 1)
                    pe.wait_ge(lnT_ready, 1)
                elif n <= FA + 1:
                    pe.wait_ge(xtl_ready, n)
                    if n >= 3:
                        pe.wait_ge(kt_ready, 2 * n - 4)
                else:
                    pe.wait_ge(kn_ready, 2 * n)
                transposes(banks[:, t1_bank(n), :], lambda c: src[:, c * P:(c + 1) * P], DC).then_inc(xt_ps, 1)

            def keys(n, h):
                pe.wait_ge(xtl_ready, n + 1)
                if n == 0:
                    pe.wait_ge(wk_lo, h + 1)
                if n > FA + 1:
                    pe.wait_ge(kt_ready, 2 * n)
                elif n >= 2:
                    pe.wait_ge(kn_ready, 2 * (n - 1) if n <= FA else 2 * n)
                dst = banks[:, k_banks(n) + h, :]
                cols = slice(h * 512, (h + 1) * 512)
                steps = [(a, w, c) for c in range(DC) for a, w in ((xth, wkh), (xth, wkl), (xtl, wkh))]
                for i, (a, w, c) in enumerate(steps):
                    last = nc.tensor.matmul(dst, a[:, n % 2, c, :], w[:, c, cols], start=(i == 0), stop=(i == len(steps) - 1))
                last.then_inc(k_ps, 1)

            def keys_transposed(n, h):
                pe.wait_ge(kn_ready, 2 * n + h + 1)
                if h == 0:
                    if n > 0:
                        pe.wait_ge(kt_ready, 2 * n - 1)
                elif n <= FA:
                    pe.wait_ge(xtl_ready, min(n + 3, FA + 2))
                    if n == FA:
                        pe.wait_ge(kt_ready, 2 * n)
                transposes(banks[:, t2_bank(n, h), :],
                           lambda i: sk[:, n % 2, (4 * h + i) * P:(4 * h + i + 1) * P], 4).then_inc(kt_ps, 1)

            def logits(u, part):
                b, g = divmod(u, G)
                if part == 0:
                    pe.wait_ge(qbd_ready, 1)
                    pe.wait_ge(kt_ready, 2 * (FA + 1) if b == 0 else 2 * TILES)
                    pe.wait_ge(max_ready, u)
                c0, c1 = ((0, 512), (512, 1024), (1024, KW))[part]
                ins = nc.tensor.matmul(banks[:, 3 + part, 0:c1 - c0], qbd[:, u, :], knT[:, b, g, c0:c1], start=True, stop=True)
                if part == 2:
                    ins.then_inc(s_ps, 1)

            def probs_transposed(u, c):
                j0, j1 = T3[c]
                if c == 0:
                    pe.wait_ge(exp_ready, u + 1)
                pe.wait_ge(ptl_ready, 3 * u + c)
                transposes(banks[:, 6, :], lambda i: block_of(u, j0 + i)[0], j1 - j0,
                           width=block_of(u, j0)[1]).then_inc(pt_ps, 1)

            def mix(u):
                b = u // G
                if u % G == 0:
                    pe.wait_ge(xnl_ready, NT * (b + 1))
                    pe.wait_ge(lns_ready, 1)
                pe.wait_ge(o_ready, u)
                for c, (j0, j1) in enumerate(T3):
                    pe.wait_ge(ptl_ready, 3 * u + c + 1)
                    for j in range(j0, j1):
                        r = block_of(u, j)[1]
                        xh = xnh[:, b * NT + j, :] if j < NT else lnh[:, b, :]
                        xl = xnl[:, b * NT + j, :] if j < NT else lnl[:, b, :]
                        for i, (p_, x_) in enumerate(((pth, xh), (pth, xl), (ptl, xh))):
                            last = nc.tensor.matmul(banks[:, 7, 0:D], p_[0:r, j, :], x_, start=(j == 0 and i == 0),
                                                    stop=(j == NB - 1 and i == 2))
                last.then_inc(u_ps, 1)

            def mix_transposed(u):
                pe.wait_ge(un_ready, u + 1)
                transposes(banks[:, 7, D:2 * D], lambda c: un[:, c * P:(c + 1) * P], DC).then_inc(ut_ps, 1)

            def values(u):
                g = u % G
                pe.wait_ge(utl_ready, u + 1)
                if u == 0:
                    pe.wait_ge(wv_lo, 1)
                steps = [(w, a, c) for c in range(DC) for w, a in ((wvh, uth), (wvl, uth), (wvh, utl))]
                for i, (w, a, c) in enumerate(steps):
                    last = nc.tensor.matmul(banks[:, 7, 0:P], w[:, c, g * P:(g + 1) * P], a[:, c, :], start=(i == 0),
                                            stop=(i == len(steps) - 1))
                last.then_inc(o_ps, 1)

            norm_transposed(0)
            for n in range(FA + 1):
                norm_transposed(n + 1)
                keys(n, 0)
                keys(n, 1)
                if n == 2:
                    pe.wait_ge(lnT_ready, 1)
                    pe.wait_ge(w_q, 16)
                    for h in range(2):
                        for c in range(DC):
                            last = nc.tensor.matmul(banks[:, 6 + h, :], lnTf[:, c, :], wq_sb[:, c, h * 512:(h + 1) * 512],
                                                    start=(c == 0), stop=(c == DC - 1))
                        last.then_inc(q_ps, 1)
                if n == 5:
                    pe.wait_ge(qn_ready, 2)
                    for h in range(2):
                        transposes(banks[:, 6 + h, :], lambda i: qn[:, (4 * h + i) * P:(4 * h + i + 1) * P], 4).then_inc(qt_ps, 1)
                if n >= 1:
                    keys_transposed(n - 1, 0)
                    keys_transposed(n - 1, 1)
            keys_transposed(FA, 0)
            keys_transposed(FA, 1)
            for part in range(3):
                logits(0, part)
            for u in range(UNITS):
                n = FA + 1 + u
                has_keys = n < TILES
                ahead = u + 1 < UNITS and u != G - 1
                if has_keys and u == 0:
                    keys(n, 0)
                    keys(n, 1)
                probs_transposed(u, 0)
                if has_keys and u > 0:
                    keys(n, 0)
                if not has_keys and ahead:
                    logits(u + 1, 0)
                if u > 0:
                    mix_transposed(u - 1)
                if has_keys and u > 0:
                    keys(n, 1)
                probs_transposed(u, 1)
                if not has_keys and ahead:
                    logits(u + 1, 1)
                if u > 0:
                    values(u - 1)
                if has_keys and ahead:
                    logits(u + 1, 0)
                    logits(u + 1, 1)
                if ahead and not has_keys:
                    logits(u + 1, 2)
                probs_transposed(u, 2)
                if ahead and has_keys:
                    logits(u + 1, 2)
                mix(u)
                if n + 1 < TILES:
                    norm_transposed(n + 1)
                if has_keys:
                    keys_transposed(n, 0)
                    keys_transposed(n, 1)
                if u == G - 1:
                    for part in range(3):
                        logits(u + 1, part)
                if u == UNITS - 3:
                    pe.wait_ge(w_tail["ffn_a"], 32)
                    pe.wait_ge(kt_ready, 2 * TILES)
                    transposes(banks[:, 0, :], lambda i: wout1_sb[:, i, :], 4)
                    transposes(banks[:, 1, :], lambda i: wout1_sb[:, 4 + i, :], 4)
                    transposes(banks[:, 2, :], lambda i: wout2_sb[:, i, :], 2).then_inc(w1T_ps, 1)
            mix_transposed(UNITS - 1)
            values(UNITS - 1)

            pe.wait_ge(o_ready, UNITS)
            pe.wait_ge(w_tail["wout"], 16)
            pe.wait_ge(w1T_ready, 1)
            for g in range(G):
                last = nc.tensor.matmul(banks[:, 0, 0:D], oT[:, g, :], wout_sb[:, g, :], start=(g == 0), stop=(g == G - 1))
            last.then_inc(y_ps, 1)

            pe.wait_ge(h_ready, 1)
            transposes(banks[:, 1, :], lambda c: tail["t0"][:, c * P:(c + 1) * P], DC).then_inc(hT_ps, 1)
            pe.wait_ge(hT_ready, 1)
            pe.wait_ge(w_tail["qkv"], 16)
            pe.wait_ge(utl_ready, UNITS)
            for first, lhs, third, done in ((4, hq, 0, q2_ps), (2, hT, 1, k2_ps), (6, hT, 2, v2_ps)):
                for h in range(2):
                    for c in range(DC):
                        last = nc.tensor.matmul(banks[:, first + h, :], lhs[:, c, :],
                                                qkv_sb[:, c, third * INNER + h * 512:third * INNER + (h + 1) * 512],
                                                start=(c == 0), stop=(c == DC - 1))
                last.then_inc(done, 1)
            pe.wait_ge(l_ready, 1)
            pe.wait_ge(dsel_ready, 1)
            nc.tensor.matmul(banks[:, 1, D:D + H], tail["dm"], logit, start=True, stop=True).then_inc(dl_ps, 1)
            pe.wait_ge(w_ready, 1)
            cT_ps_v = banks[:, 2:4, :].rearrange("p a (c r) -> p (a c) r", r=P)
            for c in range(G):
                nc.tensor.matmul(cT_ps_v[:, c, 0:M], tail["v2"][0:M, c * P:(c + 1) * P], ident[0:M, 0:M], start=True, stop=True)
                last = nc.tensor.matmul(cT_ps_v[:, c, M:P], tail["pr"][:, c * P:(c + 1) * P], tail["sel"], start=True, stop=True)
            last.then_inc(cT_ps, 1)
            pe.wait_ge(cT_ready, 1)
            pe.wait_ge(w_tail["outk"], 16)
            pe.wait_ge(x1_ready, 1)
            for g in range(G):
                last = nc.tensor.matmul(banks[:, 0, 0:D], tail["cT"][:, g * P:(g + 1) * P], outk_sb[:, g, :],
                                        start=(g == 0), stop=(g == G - 1))
            last.then_inc(y2_ps, 1)

            pe.wait_ge(f_ready, 1)
            transposes(banks[:, 1, :], lambda c: tail["t0"][:, c * P:(c + 1) * P], DC).then_inc(fT_ps, 1)
            pe.wait_ge(fT_ready, 1)
            pe.wait_ge(w_tail["c"], 48)
            pe.wait_ge(w_tail["ffn_b"], 32)
            for c in range(DC):
                last = nc.tensor.matmul(banks[:, 2, 0:E], hT[:, c, :], proj_sb[:, c, :], start=(c == 0), stop=(c == DC - 1))
            last.then_inc(e_ps, 1)
            for c in range(DC):
                last = nc.tensor.matmul(banks[:, 3, 0:P], win1_sb[:, c, :], hT[:, c, :], start=(c == 0), stop=(c == DC - 1))
            last.then_inc(z1_ps, 1)
            pe.wait_ge(a_ready, 1)
            nc.tensor.transpose(banks[0:E, 4, 0:P], zz, ident[:, :]).then_inc(aT_ps, 1)
            pe.wait_ge(aT_ready, 1)
            for i in range(2):
                nc.tensor.matmul(banks[:, 5 + i, 0:P], cw[0:E, i * R:(i + 1) * R], tail["aT"][0:E, :], start=True,
                                 stop=True).then_inc(g_ps, 1)
            pe.wait_ge(zg1_ready, 1)
            for o in range(OC):
                last = nc.tensor.matmul(banks[:, o // 4, (o % 4) * P:(o % 4 + 1) * P], wout1T[:, o * P:(o + 1) * P],
                                        tail["z1"], start=True, stop=True)
                if o % 4 == 3:
                    last.then_inc(h1_ps, 1)
            for o in range(OC):
                pe.wait_ge(h1_ready, o // 4 + 1)
                last = nc.tensor.matmul(banks[:, 3, 0:P], win2_sb[:, o, :], tail["hg"][:, o * P:(o + 1) * P],
                                        start=(o == 0), stop=(o == OC - 1))
            last.then_inc(z2_ps, 1)
            pe.wait_ge(zg2_ready, 1)
            nc.tensor.matmul(banks[:, 2, 0:D], tail["zg"], wout2T, start=True, stop=True).then_inc(f_ps, 1)


_NAMES = ["x", "ctx_1024", "mask_BxS2_bf1", "L0_xattn_ln_x_g", "L0_xattn_ln_x_b", "L0_xattn_ln_l_g", "L0_xattn_ln_l_b",
          "L0_xattn_qn_g", "L0_xattn_kn_g", "L0_xattn_Wq", "L0_xattn_Wkv", "L0_xattn_Wout", "L0_xattn_bout",
          "L0_attn_ln_scale", "L0_attn_ln_bias", "L0_attn_qkv_kernel", "L0_attn_out_kernel", "L0_ffn_proj", "L0_ffn_C1",
          "L0_ffn_Win1", "L0_ffn_Wout1", "L0_ffn_C2", "L0_ffn_Win2", "L0_ffn_Wout2"]


def kernel(**inputs):
    import numpy as np
    import concourse.bacc as bacc
    from concourse.bass_utils import run_bass_kernel_spmd

    nc = bacc.Bacc("TRN2", target_bir_lowering=False, num_devices=1)
    arrays, args = {}, []
    for name in _NAMES:
        a = np.ascontiguousarray(inputs[name])
        if a.dtype == np.bool_:
            a = a.view(np.uint8)
        arrays[f"in_{name}"] = a
        args.append(nc.dram_tensor(f"in_{name}", a.shape, mybir.dt.from_np(a.dtype), kind="ExternalInput").ap())
    shape = np.shape(inputs["x"])
    args.append(nc.dram_tensor("out_0", shape, F32, kind="ExternalOutput").ap())
    perceiver_layer(nc, *args)
    r = run_bass_kernel_spmd(nc, [arrays], core_ids=[0])
    return r.results[0]["out_0"]
```
